# Optimizing a Trainium2 kernel written in Bass

```python
import numpy as np
import jax
import jax.numpy as jnp

def _softmax(x, axis=-1):
    return jax.nn.softmax(x, axis=axis)

def _gelu(x):
    return jax.nn.gelu(x, approximate=True)

def _silu(x):
    return jax.nn.silu(x)

def _sigmoid(x):
    return jax.nn.sigmoid(x)

def _layernorm(x, axis=-1, eps=1e-05):
    m = jnp.mean(x, axis=axis, keepdims=True)
    v = jnp.var(x, axis=axis, keepdims=True)
    return (x - m) / jnp.sqrt(v + eps)

def _scatter_add(tgt, idx, src, axis=0):
    return tgt.at[idx].add(src)

def _segment_sum(src, seg, n):
    return jax.ops.segment_sum(src, seg, n)
kernel_name = 'mk_dlrm_tower_d1_rec_r8_3a2b06'

def setup_inputs(seed: int=0):
    np.random.seed(seed)
    _w = jnp.asarray

    def _rec_inputs():
        import jax
        import jax.numpy as jnp
        _tk = jax.random.key(seed)
        ids = jnp.stack([jax.random.randint(jax.random.fold_in(_tk, 200 + f), (512,), 0, v, jnp.int32) for f, v in enumerate([1000, 12500, 1250, 1000, 12500, 1250, 1000, 125000, 12500, 1250, 1250, 1250, 1250, 12500, 1250, 1250, 12500, 12500, 1000, 1250, 12500, 1000, 1250, 12500, 1000, 1250])], axis=1)
        tbl_0 = 0.05 * jax.random.normal(jax.random.fold_in(_tk, 500 + 0), (1000, 128), jnp.float32)
        tbl_1 = 0.05 * jax.random.normal(jax.random.fold_in(_tk, 500 + 1), (12500, 128), jnp.float32)
        tbl_2 = 0.05 * jax.random.normal(jax.random.fold_in(_tk, 500 + 2), (1250, 128), jnp.float32)
        tbl_3 = 0.05 * jax.random.normal(jax.random.fold_in(_tk, 500 + 3), (1000, 128), jnp.float32)
        tbl_4 = 0.05 * jax.random.normal(jax.random.fold_in(_tk, 500 + 4), (12500, 128), jnp.float32)
        tbl_5 = 0.05 * jax.random.normal(jax.random.fold_in(_tk, 500 + 5), (1250, 128), jnp.float32)
        tbl_6 = 0.05 * jax.random.normal(jax.random.fold_in(_tk, 500 + 6), (1000, 128), jnp.float32)
        tbl_7 = 0.05 * jax.random.normal(jax.random.fold_in(_tk, 500 + 7), (125000, 128), jnp.float32)
        tbl_8 = 0.05 * jax.random.normal(jax.random.fold_in(_tk, 500 + 8), (12500, 128), jnp.float32)
        tbl_9 = 0.05 * jax.random.normal(jax.random.fold_in(_tk, 500 + 9), (1250, 128), jnp.float32)
        tbl_10 = 0.05 * jax.random.normal(jax.random.fold_in(_tk, 500 + 10), (1250, 128), jnp.float32)
        tbl_11 = 0.05 * jax.random.normal(jax.random.fold_in(_tk, 500 + 11), (1250, 128), jnp.float32)
        tbl_12 = 0.05 * jax.random.normal(jax.random.fold_in(_tk, 500 + 12), (1250, 128), jnp.float32)
        tbl_13 = 0.05 * jax.random.normal(jax.random.fold_in(_tk, 500 + 13), (12500, 128), jnp.float32)
        tbl_14 = 0.05 * jax.random.normal(jax.random.fold_in(_tk, 500 + 14), (1250, 128), jnp.float32)
        tbl_15 = 0.05 * jax.random.normal(jax.random.fold_in(_tk, 500 + 15), (1250, 128), jnp.float32)
        tbl_16 = 0.05 * jax.random.normal(jax.random.fold_in(_tk, 500 + 16), (12500, 128), jnp.float32)
        tbl_17 = 0.05 * jax.random.normal(jax.random.fold_in(_tk, 500 + 17), (12500, 128), jnp.float32)
        tbl_18 = 0.05 * jax.random.normal(jax.random.fold_in(_tk, 500 + 18), (1000, 128), jnp.float32)
        tbl_19 = 0.05 * jax.random.normal(jax.random.fold_in(_tk, 500 + 19), (1250, 128), jnp.float32)
        tbl_20 = 0.05 * jax.random.normal(jax.random.fold_in(_tk, 500 + 20), (12500, 128), jnp.float32)
        tbl_21 = 0.05 * jax.random.normal(jax.random.fold_in(_tk, 500 + 21), (1000, 128), jnp.float32)
        tbl_22 = 0.05 * jax.random.normal(jax.random.fold_in(_tk, 500 + 22), (1250, 128), jnp.float32)
        tbl_23 = 0.05 * jax.random.normal(jax.random.fold_in(_tk, 500 + 23), (12500, 128), jnp.float32)
        tbl_24 = 0.05 * jax.random.normal(jax.random.fold_in(_tk, 500 + 24), (1000, 128), jnp.float32)
        tbl_25 = 0.05 * jax.random.normal(jax.random.fold_in(_tk, 500 + 25), (1250, 128), jnp.float32)
        _rk = jax.random.fold_in(_tk, 7)
        r_dense_features = -0.000520686 + 1.00062 * jax.random.normal(jax.random.fold_in(_rk, 101), (512, 128), jnp.float32)
        W_top1 = 0.0405887 * jax.random.normal(jax.random.fold_in(_tk, 801), (607, 512), jnp.float32)
        W_top2 = 0.0441942 * jax.random.normal(jax.random.fold_in(_tk, 802), (512, 256), jnp.float32)
        W_top3 = 0.0625 * jax.random.normal(jax.random.fold_in(_tk, 803), (256, 1), jnp.float32)
        b_top1 = jnp.zeros((512,), jnp.float32)
        b_top2 = jnp.zeros((256,), jnp.float32)
        return (r_dense_features, ids, tbl_0, tbl_1, tbl_2, tbl_3, tbl_4, tbl_5, tbl_6, tbl_7, tbl_8, tbl_9, tbl_10, tbl_11, tbl_12, tbl_13, tbl_14, tbl_15, tbl_16, tbl_17, tbl_18, tbl_19, tbl_20, tbl_21, tbl_22, tbl_23, tbl_24, tbl_25, W_top1, b_top1, W_top2, b_top2, W_top3)
    r_dense_features, ids, tbl_0, tbl_1, tbl_2, tbl_3, tbl_4, tbl_5, tbl_6, tbl_7, tbl_8, tbl_9, tbl_10, tbl_11, tbl_12, tbl_13, tbl_14, tbl_15, tbl_16, tbl_17, tbl_18, tbl_19, tbl_20, tbl_21, tbl_22, tbl_23, tbl_24, tbl_25, W_top1, b_top1, W_top2, b_top2, W_top3 = _rec_inputs()

    def _L0_rec_setup():
        import jax, jax.numpy as jnp
        import numpy as np
        F = 26
        N = F + 1
        _TRIU_I, _TRIU_J = np.triu_indices(N, k=1)
        key = jax.random.key(seed)
        k1, k2 = jax.random.split(key)
        B, D = (2048, 128)
        dense_features = jax.random.normal(k1, (B, D), dtype=jnp.float32)
        sparse_features = jax.random.normal(k2, (B, F, D), dtype=jnp.float32)
        return {'dense_features': dense_features, 'sparse_features': sparse_features}
    _L0_rec_all = _L0_rec_setup()
    _L0_rec_in = {k: v for k, v in _L0_rec_all.items() if k in ()}
    del _L0_rec_all
    return {'r_dense_features': r_dense_features, 'ids': ids, 'tbl_0': tbl_0, 'tbl_1': tbl_1, 'tbl_2': tbl_2, 'tbl_3': tbl_3, 'tbl_4': tbl_4, 'tbl_5': tbl_5, 'tbl_6': tbl_6, 'tbl_7': tbl_7, 'tbl_8': tbl_8, 'tbl_9': tbl_9, 'tbl_10': tbl_10, 'tbl_11': tbl_11, 'tbl_12': tbl_12, 'tbl_13': tbl_13, 'tbl_14': tbl_14, 'tbl_15': tbl_15, 'tbl_16': tbl_16, 'tbl_17': tbl_17, 'tbl_18': tbl_18, 'tbl_19': tbl_19, 'tbl_20': tbl_20, 'tbl_21': tbl_21, 'tbl_22': tbl_22, 'tbl_23': tbl_23, 'tbl_24': tbl_24, 'tbl_25': tbl_25, 'W_top1': W_top1, 'b_top1': b_top1, 'W_top2': W_top2, 'b_top2': b_top2, 'W_top3': W_top3}

def reference(r_dense_features, ids, tbl_0, tbl_1, tbl_2, tbl_3, tbl_4, tbl_5, tbl_6, tbl_7, tbl_8, tbl_9, tbl_10, tbl_11, tbl_12, tbl_13, tbl_14, tbl_15, tbl_16, tbl_17, tbl_18, tbl_19, tbl_20, tbl_21, tbl_22, tbl_23, tbl_24, tbl_25, W_top1, b_top1, W_top2, b_top2, W_top3):
    import jax
    import jax.numpy as jnp

    def _L0_rec_ref(dense_features, sparse_features):
        import jax, jax.numpy as jnp
        import numpy as np
        F = 26
        N = F + 1
        _TRIU_I, _TRIU_J = np.triu_indices(N, k=1)
        combined = jnp.concatenate([dense_features[:, None, :], sparse_features], axis=1)
        interactions = jnp.einsum('bnd,bmd->bnm', combined, combined)
        interactions_flat = interactions[:, _TRIU_I, _TRIU_J]
        return jnp.concatenate([dense_features, interactions_flat], axis=1)
    e = jnp.stack([tbl_0[ids[:, 0]], tbl_1[ids[:, 1]], tbl_2[ids[:, 2]], tbl_3[ids[:, 3]], tbl_4[ids[:, 4]], tbl_5[ids[:, 5]], tbl_6[ids[:, 6]], tbl_7[ids[:, 7]], tbl_8[ids[:, 8]], tbl_9[ids[:, 9]], tbl_10[ids[:, 10]], tbl_11[ids[:, 11]], tbl_12[ids[:, 12]], tbl_13[ids[:, 13]], tbl_14[ids[:, 14]], tbl_15[ids[:, 15]], tbl_16[ids[:, 16]], tbl_17[ids[:, 17]], tbl_18[ids[:, 18]], tbl_19[ids[:, 19]], tbl_20[ids[:, 20]], tbl_21[ids[:, 21]], tbl_22[ids[:, 22]], tbl_23[ids[:, 23]], tbl_24[ids[:, 24]], tbl_25[ids[:, 25]]], axis=1)
    z = _L0_rec_ref(r_dense_features, e)
    z = z.reshape(z.shape[0], -1)
    h = jnp.concatenate([z, r_dense_features], axis=1)
    h = jnp.maximum(h @ W_top1 + b_top1, 0.0)
    h = jnp.maximum(h @ W_top2 + b_top2, 0.0)
    y = h @ W_top3
    return y

_drawn_inputs = setup_inputs


def setup_inputs(seed=0):
    import zlib

    import numpy as np

    out = dict(_drawn_inputs(seed))
    spreads = {'b_top1': (0.0, 0.1), 'b_top2': (0.0, 0.1)}
    factors = {}
    for name, (base, spread) in spreads.items():
        noise = np.random.default_rng([zlib.crc32(name.encode()), seed]).standard_normal(out[name].shape)
        drawn = base * np.exp(spread * noise) if base else spread * noise
        out[name] = jnp.asarray(drawn.astype(out[name].dtype))
    for name, factor in factors.items():
        out[name] = (out[name] * factor).astype(out[name].dtype)
    return out
```

```python
import numpy as np
import concourse.bass as bass
from concourse import mybir
from contextlib import ExitStack

FP32 = mybir.dt.float32
INT32 = mybir.dt.int32
UINT32 = mybir.dt.uint32
ACT = mybir.ActivationFunctionType
ALU = mybir.AluOpType

P = 128
B = 512
D = 128
TABLES = 26
N = TABLES + 1
NPAD = 32
H1, H2 = 512, 256
PAIRS = N * (N - 1) // 2
TILES = B // P
HALF = (N - 1) // 2
VECS = HALF + 1
QUADS = P // NPAD
VEC_SLOTS = -(-VECS // QUADS)
FILL = 4
FILLS = -(-N // FILL)
GROUP = P // NPAD
BANK = 512
GROUPS_PER_BANK = BANK // (GROUP * N)
ROUND_BANKS = 2
ROUND = ROUND_BANKS * GROUPS_PER_BANK
ROUNDS = P // GROUP // ROUND
F1 = H1 // P
F2 = H2 // P


def pair_row(a, b):
    a, b = min(a, b), max(a, b)
    return D + a * N - a * (a + 1) // 2 + (b - a - 1)


def interaction_rows():
    zero = D + PAIRS + D
    rows = np.full((P, VEC_SLOTS), zero)
    for t in range(VECS):
        for m in range(N):
            low = t < HALF and t < m <= t + HALF
            n = t if low else t + HALF
            if m != n and m != t and (t < HALF or m < HALF):
                rows[(t % QUADS) * NPAD + m, t // QUADS] = pair_row(n, m)
    return rows


def dlrm_tower(nc, dense, ids, tables, w1_pairs, w1_dense, b1, w2, b2, w3, ident, low_mask, out):
    ctx = ExitStack()
    with ctx:
        def sb(name, shape, dt=FP32):
            return ctx.enter_context(nc.sbuf_tensor(name, shape, dt))

        def pb(name, shape):
            return ctx.enter_context(nc.psum_tensor(name, shape, FP32))

        def sem(name):
            return ctx.enter_context(nc.semaphore(name))

        ids_sb = sb("ids_sb", [P, TILES, TABLES], INT32)
        dense_sb = sb("dense_sb", [P, TILES, D])
        rows_sb = sb("rows_sb", [P, TILES, TABLES, D])
        ident_sb = sb("ident_sb", [P, P])
        mask_sb = sb("mask_sb", [P, HALF], INT32)
        w1p_sb = sb("w1p_sb", [P, VEC_SLOTS, H1])
        w1d_sb = sb("w1d_sb", [P, 2, H1])
        w1dsum_sb = sb("w1dsum_sb", [P, H1])
        w2_sb = sb("w2_sb", [P, F1, H2])
        w3_sb = sb("w3_sb", [P, F2])
        b1_sb = sb("b1_sb", [P, F1])
        b2_sb = sb("b2_sb", [P, F2])
        feats = sb("feats", [P, B, NPAD])
        vecs = sb("vecs", [P, 2, VECS, P // GROUP])
        pairs = sb("pairs", [P, VEC_SLOTS, B])
        h1_sb = sb("h1_sb", [P, 2, F1, P])
        h2_sb = sb("h2_sb", [P, 2, F2, P])
        y_sb = sb("y_sb", [1, B])

        turn_ps = [pb(f"turn_ps{i}", [P, FILL, P]) for i in range(2)]
        gram_ps = [pb(f"gram_ps{i}", [P, ROUND_BANKS, BANK]) for i in range(2)]
        h1_ps = pb("h1_ps", [P, F1, P])
        tail_ps = pb("tail_ps", [P, BANK])
        h2_ps = tail_ps[:, 0:H2].rearrange("p (f b) -> p f b", f=F2)
        y_ps = tail_ps[0:1, H2:H2 + P]

        ids_loaded = sem("ids_loaded")
        ident_loaded = sem("ident_loaded")
        dense_loaded = sem("dense_loaded")
        mask_loaded = sem("mask_loaded")
        w1p_loaded = sem("w1p_loaded")
        w1d_loaded = sem("w1d_loaded")
        w2_loaded = sem("w2_loaded")
        small_loaded = sem("small_loaded")
        rows_gathered = [[sem(f"rows_gathered{t}_{k}") for k in range(FILLS)] for t in range(TILES)]
        pad_zeroed = sem("pad_zeroed")
        w1d_summed = sem("w1d_summed")
        turned = sem("turned")
        copied_act = sem("copied_act")
        copied_dve = sem("copied_dve")
        gram_done = sem("gram_done")
        high_taken = sem("high_taken")
        low_taken = sem("low_taken")
        pairs_placed = sem("pairs_placed")
        h1_done = sem("h1_done")
        h1_relu = sem("h1_relu")
        h2_done = sem("h2_done")
        h2_relu = sem("h2_relu")
        y_done = sem("y_done")
        y_copied = sem("y_copied")
        y_stored = sem("y_stored")

        def fill_features(k):
            return range(FILL * k, min(FILL * (k + 1), N))

        def fills_to(tile, k, engine):
            return (tile * FILLS + k + 1 + 1 - engine) // 2

        block = ctx.enter_context(nc.Block())

        @block.sync
        def _(sp):
            sp.dma_start(ids_sb[:, :, :], ids).then_inc(ids_loaded, 16)
            sp.dma_start(ident_sb[:, :], ident).then_inc(ident_loaded, 16)
            sp.dma_start(dense_sb[:, :, :], dense).then_inc(dense_loaded, 16)
            sp.dma_start(mask_sb[:, :], low_mask).then_inc(mask_loaded, 16)
            sp.dma_start(w1d_sb[:, :, :], w1_dense).then_inc(w1d_loaded, 16)
            sp.dma_start(w1p_sb[:, :, :], w1_pairs).then_inc(w1p_loaded, 16)
            sp.dma_start(w2_sb[:, :, :], w2).then_inc(w2_loaded, 16)
            sp.dma_start(b1_sb[:, :], b1).then_inc(small_loaded, 16)
            sp.dma_start(b2_sb[:, :], b2).then_inc(small_loaded, 16)
            sp.dma_start(w3_sb[:, :], w3).then_inc(small_loaded, 16)
            sp.wait_ge(y_copied, TILES)
            sp.dma_start(out, y_sb[:, :]).then_inc(y_stored, 16)
            sp.wait_ge(y_stored, 16)

        @block.gpsimd
        def _(pool):
            pool.wait_ge(ids_loaded, 16)
            for tile in range(TILES):
                for k in range(FILLS):
                    for n in fill_features(k):
                        if n > 0:
                            pool.indirect_dma_start(
                                out=rows_sb[:, tile, n - 1, :], out_offset=None,
                                in_=tables[n - 1],
                                in_offset=bass.IndirectOffsetOnAxis(
                                    ids_sb[:, tile, n - 1:n].bitcast(UINT32), 0),
                            ).then_inc(rows_gathered[tile][k], 16)

        @block.tensor
        def _(pe):
            def transposes(tile, k):
                i = tile * FILLS + k
                if i == 0:
                    pe.wait_ge(ident_loaded, 16)
                    pe.wait_ge(dense_loaded, 16)
                pe.wait_ge(rows_gathered[tile][k], 16 * sum(n > 0 for n in fill_features(k)))
                if i >= 2:
                    pe.wait_ge(copied_dve if i % 2 else copied_act, i // 2)
                for n in fill_features(k):
                    block_in = rows_sb[:, tile, n - 1, :] if n else dense_sb[:, tile, :]
                    last = nc.tensor.transpose(turn_ps[i % 2][:, n - FILL * k, :], block_in, ident_sb[:, :])
                last.then_inc(turned, 1)

            def gram_round(tile, r):
                i = tile * ROUNDS + r
                if r == 0:
                    pe.wait_ge(copied_act, fills_to(tile, FILLS - 1, 0))
                    pe.wait_ge(copied_dve, fills_to(tile, FILLS - 1, 1))
                    if tile == 0:
                        pe.wait_ge(pad_zeroed, 1)
                if i >= 2:
                    pe.wait_ge(low_taken, i - 1)
                for g in range(ROUND):
                    b = tile * P + (r * ROUND + g) * GROUP
                    c = g % GROUPS_PER_BANK * GROUP * N
                    last = nc.tensor.matmul(
                        gram_ps[i % 2][:, g // GROUPS_PER_BANK, c:c + GROUP * N],
                        feats[:, b:b + GROUP, :], feats[:, b:b + GROUP, 0:N], start=True, stop=True)
                last.then_inc(gram_done, 1)

            def layer1(tile):
                cols = slice(tile * P, (tile + 1) * P)
                pe.wait_ge(pairs_placed, tile + 1)
                if tile == 0:
                    pe.wait_ge(w1p_loaded, 16)
                    pe.wait_ge(w1d_summed, 1)
                else:
                    pe.wait_ge(h1_relu, tile)
                for f in range(F1):
                    fs = slice(f * P, (f + 1) * P)
                    nc.tensor.matmul(h1_ps[:, f, :], w1dsum_sb[:, fs], feats[:, cols, 0], start=True, stop=False)
                    for s in range(VEC_SLOTS):
                        k = min(QUADS, VECS - s * QUADS) * NPAD
                        last = nc.tensor.matmul(h1_ps[:, f, :], w1p_sb[0:k, s, fs], pairs[0:k, s, cols],
                                                start=False, stop=s == VEC_SLOTS - 1)
                last.then_inc(h1_done, 1)

            def layer2(tile):
                pe.wait_ge(h1_relu, tile + 1)
                if tile == 0:
                    pe.wait_ge(w2_loaded, 16)
                else:
                    pe.wait_ge(h2_relu, tile)
                    pe.wait_ge(y_copied, tile)
                for c in range(F2):
                    for f in range(F1):
                        last = nc.tensor.matmul(h2_ps[:, c, :], w2_sb[:, f, c * P:(c + 1) * P],
                                                h1_sb[:, tile % 2, f, :], start=f == 0, stop=f == F1 - 1)
                last.then_inc(h2_done, 1)

            def layer3(tile):
                pe.wait_ge(h2_relu, tile + 1)
                if tile == 0:
                    pe.wait_ge(small_loaded, 48)
                for c in range(F2):
                    last = nc.tensor.matmul(y_ps, w3_sb[:, c:c + 1], h2_sb[:, tile % 2, c, :],
                                            start=c == 0, stop=c == F2 - 1)
                last.then_inc(y_done, 1)

            stages = [lambda t, r=r: gram_round(t, r) for r in range(ROUNDS)] + [layer1, layer2, layer3]
            for k in range(FILLS):
                transposes(0, k)
            for tile in range(TILES):
                for k, stage in enumerate(stages):
                    stage(tile)
                    if tile + 1 < TILES:
                        transposes(tile + 1, k)

        def copy_fill(engine, copy, copied, tile, k):
            n0, width = FILL * k, len(fill_features(k))
            return copy(feats[:, tile * P:(tile + 1) * P, n0:n0 + width].rearrange("p b n -> p n b"),
                        turn_ps[(tile * FILLS + k) % 2][:, 0:width, :])

        def gram_columns(i, quad, first, count):
            at = gram_ps[i % 2][quad * NPAD:(quad + 1) * NPAD, :, 0:GROUPS_PER_BANK * GROUP * N]
            at = at.rearrange("p k (g c) -> p k g c", c=GROUP * N)
            return at[:, :, :, quad * N + first:quad * N + first + count]

        def vec_places(i, quad, count):
            tile, r = divmod(i, ROUNDS)
            at = vecs[quad * NPAD:(quad + 1) * NPAD, tile % 2, 0:count, r * ROUND:(r + 1) * ROUND]
            return at.rearrange("p t (k g) -> p k g t", k=ROUND_BANKS)

        @block.scalar
        def _(act):
            def fill(tile, k):
                i = tile * FILLS + k
                if i % 2 == 0:
                    act.wait_ge(turned, i + 1)
                    copy_fill(act, nc.scalar.copy, copied_act, tile, k).then_inc(copied_act, 1)

            def take_high(tile, r):
                i = tile * ROUNDS + r
                act.wait_ge(gram_done, i + 1)
                if r == 0 and tile >= 2:
                    act.wait_ge(pairs_placed, tile - 1)
                for q in range(QUADS):
                    last = nc.scalar.copy(vec_places(i, q, VECS), gram_columns(i, q, HALF, VECS))
                last.then_inc(high_taken, 1)

            def copy_y(tile):
                act.wait_ge(y_done, tile + 1)
                nc.scalar.copy(y_sb[:, tile * P:(tile + 1) * P], y_ps).then_inc(y_copied, 1)

            stages = [lambda t, r=r: take_high(t, r) for r in range(ROUNDS)] + [lambda t: None, lambda t: None, copy_y]
            for k in range(FILLS):
                fill(0, k)
            for tile in range(TILES):
                for k, stage in enumerate(stages):
                    stage(tile)
                    if tile + 1 < TILES:
                        fill(tile + 1, k)

        @block.vector
        def _(dve):
            nc.vector.memset(feats[:, :, N:NPAD], 0.0).then_inc(pad_zeroed, 1)
            dve.wait_ge(w1d_loaded, 16)
            nc.vector.tensor_tensor(w1dsum_sb[:, :], w1d_sb[:, 0, :], w1d_sb[:, 1, :], ALU.add).then_inc(w1d_summed, 1)
            dve.wait_ge(mask_loaded, 16)

            def fill(tile, k):
                i = tile * FILLS + k
                if i % 2 == 1:
                    dve.wait_ge(turned, i + 1)
                    copy_fill(dve, nc.vector.tensor_copy, copied_dve, tile, k).then_inc(copied_dve, 1)

            def take_low(tile, r):
                i = tile * ROUNDS + r
                dve.wait_ge(high_taken, i + 1)
                for q in range(QUADS):
                    where = mask_sb[q * NPAD:(q + 1) * NPAD, :].unsqueeze(1).unsqueeze(1)
                    where = where.to_broadcast([NPAD, ROUND_BANKS, GROUPS_PER_BANK, HALF])
                    last = nc.vector.copy_predicated(vec_places(i, q, HALF), where, gram_columns(i, q, 0, HALF))
                last.then_inc(low_taken, 1)

            def place(tile):
                dve.wait_ge(low_taken, (tile + 1) * ROUNDS)
                for to in range(QUADS):
                    count = len(range(to, VECS, QUADS))
                    for q in range(QUADS):
                        last = nc.vector.tensor_copy(
                            pairs[to * NPAD:(to + 1) * NPAD, 0:count, tile * P + q:(tile + 1) * P:GROUP],
                            vecs[q * NPAD:(q + 1) * NPAD, tile % 2, to:VECS:QUADS, :])
                last.then_inc(pairs_placed, 1)

            def relu1(tile):
                dve.wait_ge(h1_done, tile + 1)
                if tile == 0:
                    dve.wait_ge(small_loaded, 48)
                if tile >= 2:
                    dve.wait_ge(h2_done, tile - 1)
                for f in range(F1):
                    last = nc.vector.tensor_scalar(h1_sb[:, tile % 2, f, :], h1_ps[:, f, :],
                                                   b1_sb[:, f:f + 1], 0.0, ALU.add, ALU.max)
                last.then_inc(h1_relu, 1)

            def relu2(tile):
                dve.wait_ge(h2_done, tile + 1)
                if tile >= 2:
                    dve.wait_ge(y_done, tile - 1)
                for c in range(F2):
                    last = nc.vector.tensor_scalar(h2_sb[:, tile % 2, c, :], h2_ps[:, c, :],
                                                   b2_sb[:, c:c + 1], 0.0, ALU.add, ALU.max)
                last.then_inc(h2_relu, 1)

            def last_round(tile):
                take_low(tile, ROUNDS - 1)
                place(tile)

            stages = [lambda t, r=r: take_low(t, r) for r in range(ROUNDS - 1)]
            stages += [last_round, relu1, relu2, lambda t: None]
            for k in range(FILLS):
                fill(0, k)
            for tile in range(TILES):
                for k, stage in enumerate(stages):
                    stage(tile)
                    if tile + 1 < TILES:
                        fill(tile + 1, k)


def kernel(**inputs):
    import concourse.bacc as bacc
    from concourse.bass_utils import run_bass_kernel_spmd

    w1 = np.asarray(inputs["W_top1"])
    w1_padded = np.concatenate([w1, np.zeros((1, H1), w1.dtype)])
    m = np.arange(P)[:, None] % NPAD
    t = np.arange(HALF)[None, :]
    by_tile = lambda a: np.ascontiguousarray(np.asarray(a).reshape(TILES, P, -1).transpose(1, 0, 2))
    by_chunk = lambda a, c: np.ascontiguousarray(np.asarray(a).reshape(c, P, -1).transpose(1, 0, 2))
    arrays = {
        "dense": by_tile(inputs["r_dense_features"]),
        "ids": by_tile(inputs["ids"]),
        "w1_pairs": w1_padded[interaction_rows()],
        "w1_dense": np.ascontiguousarray(np.stack([w1[:D], w1[D + PAIRS:]], axis=1)),
        "b1": np.ascontiguousarray(np.asarray(inputs["b_top1"]).reshape(F1, P).T),
        "w2": by_chunk(inputs["W_top2"], F1),
        "b2": np.ascontiguousarray(np.asarray(inputs["b_top2"]).reshape(F2, P).T),
        "w3": np.ascontiguousarray(np.asarray(inputs["W_top3"]).reshape(F2, P).T),
        "ident": np.eye(P, dtype=np.float32),
        "low_mask": ((m > t) & (m <= t + HALF)).astype(np.int32),
    }
    for f in range(TABLES):
        arrays[f"tbl_{f}"] = np.ascontiguousarray(inputs[f"tbl_{f}"])

    nc = bacc.Bacc("TRN2", target_bir_lowering=False, num_devices=1)
    aps = {name: nc.dram_tensor(f"in_{name}", a.shape, mybir.dt.from_np(a.dtype), kind="ExternalInput").ap()
           for name, a in arrays.items()}
    out = nc.dram_tensor("y", (1, B), FP32, kind="ExternalOutput").ap()
    tables = [aps.pop(f"tbl_{f}") for f in range(TABLES)]
    dlrm_tower(nc, tables=tables, out=out, **aps)
    result = run_bass_kernel_spmd(nc, [{f"in_{name}": a for name, a in arrays.items()}], core_ids=[0])
    return result.results[0]["y"].reshape(B, 1)
```

```python
import numpy as np
import concourse.bass as bass
from concourse import mybir
from contextlib import ExitStack

FP32 = mybir.dt.float32
FP32R = mybir.dt.float32r
INT32 = mybir.dt.int32
UINT32 = mybir.dt.uint32
ACT = mybir.ActivationFunctionType
ALU = mybir.AluOpType

P = 128
B = 512
D = 128
TABLE_ROWS = [1000, 12500, 1250, 1000, 12500, 1250, 1000, 125000, 12500, 1250, 1250, 1250, 1250,
              12500, 1250, 1250, 12500, 12500, 1000, 1250, 12500, 1000, 1250, 12500, 1000, 1250]
TABLES = len(TABLE_ROWS)
N = TABLES + 1
NPAD = 32
H1, H2 = 512, 256
F1, F2 = H1 // P, H2 // P
PAIRS = N * (N - 1) // 2
TILES = B // P
QUADS = P // NPAD

LOOKUPS = 6
BY_SIZE = sorted(range(TABLES), key=lambda f: TABLE_ROWS[f])
LOOKED_UP = BY_SIZE[:LOOKUPS]
GATHERED = sorted(BY_SIZE[LOOKUPS:])
SLOT_FEATURES = [f + 1 for f in LOOKED_UP] + [0] + [f + 1 for f in GATHERED]
DENSE_SLOT = LOOKUPS

FILL = 4
HALF = (N - 1) // 2
VECS = HALF + 1
VEC_SLOTS = -(-VECS // QUADS)
FILLS = -(-(N - LOOKUPS) // FILL)
FILL_SLOTS = [range(max(LOOKUPS, N - FILL * (FILLS - k)), N - FILL * (FILLS - k - 1)) for k in range(FILLS)]

GROUP = P // NPAD
GROUPS = P // GROUP
BANK = 512
ROUND_BANKS = 2
GROUPS_PER_BANK = BANK // (GROUP * N)
ROUND = ROUND_BANKS * GROUPS_PER_BANK
ROUNDS = GROUPS // ROUND
CHUNKS = [-(-TABLE_ROWS[f] // P) for f in LOOKED_UP]
CHUNKS_MAX = max(CHUNKS)
CHUNK_BASE = [sum(CHUNKS[:u]) for u in range(LOOKUPS + 1)]
TABLE_BUFS = 3
ONEHOTS = 12
LOOKUP_PS = 2
ACT_QUADS = 1
ACT_CHUNKS = 2


def dve_chunks(u):
    n = CHUNKS[u] - ACT_CHUNKS
    return [range(0, n // 2), range(n // 2, n)]


def ring_runs(first, end):
    seam = -(-first // ONEHOTS) * ONEHOTS
    return [(first, seam), (seam, end)] if first < seam < end else [(first, end)]


def chunk_rows(u, c):
    full = CHUNKS[u] - 1
    return P if c < full else TABLE_ROWS[LOOKED_UP[u]] - full * P


def chunk_row_ids():
    p = np.arange(P)
    columns = [p * (CHUNKS[u] - 1) + c if c < CHUNKS[u] - 1 else p + P * c
               for u in range(LOOKUPS) for c in range(CHUNKS[u])]
    return np.stack(columns, axis=1).astype(np.float32)


def pair_row(a, b):
    a, b = min(a, b), max(a, b)
    return D + a * N - a * (a + 1) // 2 + (b - a - 1)


def interaction_rows():
    rows = np.full((P, VEC_SLOTS), D + PAIRS + D)
    for t in range(VECS):
        for m in range(N):
            n = t if t < HALF and t < m <= t + HALF else t + HALF
            if m != n and m != t and (t < HALF or m < HALF):
                rows[(t % QUADS) * NPAD + m, t // QUADS] = pair_row(SLOT_FEATURES[n], SLOT_FEATURES[m])
    return rows


def dlrm_tower(nc, dense, ids, lookup_ids, row_ids, tables, w1_pairs, w1_dense, w2, w3, b1, b2,
               ident, low_mask, out):
    ctx = ExitStack()
    with ctx:
        def sb(name, shape, dt=FP32):
            return ctx.enter_context(nc.sbuf_tensor(name, shape, dt))

        def pb(name, shape):
            return ctx.enter_context(nc.psum_tensor(name, shape, FP32))

        def sem(name):
            return ctx.enter_context(nc.semaphore(name))

        ids_sb = sb("ids_sb", [P, TILES, TABLES], INT32)
        dense_sb = sb("dense_sb", [P, TILES, D])
        rows_sb = sb("rows_sb", [P, TILES, len(GATHERED), D])
        table_sb = sb("table_sb", [P, TABLE_BUFS, CHUNKS_MAX, D])
        lookup_ids_sb = sb("lookup_ids_sb", [P, TABLE_BUFS, B], INT32)
        high_sb = sb("high_sb", [P, 2, CHUNKS_MAX, D], FP32R)
        low_sb = sb("low_sb", [P, 2, CHUNKS_MAX, D], FP32R)
        row_ids_sb = sb("row_ids_sb", [P, CHUNK_BASE[LOOKUPS]])
        onehot_sb = sb("onehot_sb", [P, ONEHOTS, B], FP32R)
        distance_sb = sb("distance_sb", [P, ACT_CHUNKS, B])
        ident_sb = sb("ident_sb", [P, P])
        mask_sb = sb("mask_sb", [P, HALF], INT32)
        w1p_sb = sb("w1p_sb", [P, VEC_SLOTS, H1])
        w1d_sb = sb("w1d_sb", [P, 2, H1])
        w2_sb = sb("w2_sb", [P, F1, H2])
        w3_sb = sb("w3_sb", [P, F2])
        b1_sb = sb("b1_sb", [P, F1])
        b2_sb = sb("b2_sb", [P, F2])
        feats = sb("feats", [P, B, NPAD])
        vecs = sb("vecs", [P, 2, VECS, GROUPS])
        pairs = sb("pairs", [P, VEC_SLOTS, B])
        h1_sb = sb("h1_sb", [P, F1, P])
        h2_sb = sb("h2_sb", [P, F2, P])
        y_sb = sb("y_sb", [1, B])

        turn_ps = [pb(f"turn_ps{i}", [P, FILL, P]) for i in range(2)]
        gram_ps = [pb(f"gram_ps{i}", [P, ROUND_BANKS, BANK]) for i in range(2)]
        ids_ps = gram_ps[1]
        h1_ps = pb("h1_ps", [P, F1, P])
        tail_ps = pb("tail_ps", [P, BANK])
        h2_ps = tail_ps[:, 0:H2].rearrange("p (f b) -> p f b", f=F2)
        y_ps = tail_ps[0:1, H2:H2 + P]

        ids_loaded = sem("ids_loaded")
        ident_loaded = sem("ident_loaded")
        dense_loaded = sem("dense_loaded")
        mask_loaded = sem("mask_loaded")
        row_ids_loaded = sem("row_ids_loaded")
        lookup_ids_loaded = [sem(f"lookup_ids_loaded{u}") for u in range(LOOKUPS)]
        table_loaded = [sem(f"table_loaded{u}") for u in range(LOOKUPS)]
        w1p_loaded = sem("w1p_loaded")
        w1d_loaded = sem("w1d_loaded")
        w2_loaded = sem("w2_loaded")
        small_loaded = sem("small_loaded")
        rows_gathered = [[sem(f"rows_gathered{t}_{k}") for k in range(FILLS)] for t in range(TILES)]
        ids_in_psum = sem("ids_in_psum")
        high_split = sem("high_split")
        low_split = sem("low_split")
        distance_made = sem("distance_made")
        onehot_dve = sem("onehot_dve")
        onehot_act = sem("onehot_act")
        chunk_used = sem("chunk_used")
        slots_zeroed = sem("slots_zeroed")
        w1d_summed = sem("w1d_summed")
        turned = sem("turned")
        copied_act = sem("copied_act")
        copied_dve = sem("copied_dve")
        gram_done = sem("gram_done")
        high_taken = sem("high_taken")
        low_taken = sem("low_taken")
        placed_act = sem("placed_act")
        placed_dve = sem("placed_dve")
        h1_done = sem("h1_done")
        h1_relu = sem("h1_relu")
        h2_done = sem("h2_done")
        h2_relu = sem("h2_relu")
        y_done = sem("y_done")
        y_copied = sem("y_copied")
        y_stored = sem("y_stored")

        plan = []
        for u in range(max(LOOKUPS, FILLS)):
            if u < LOOKUPS:
                plan.append(("lookup", u, 0, "act"))
            if u < FILLS:
                plan.append(("turn", 0, u, "act"))
        first_tile_fills = len(plan)
        for tile in range(1, TILES):
            for k in range(FILLS):
                plan.append(("turn", tile, k, "act" if k % 2 else "dve"))
        copied = {"act": copied_act, "dve": copied_dve}

        def plan_index(tile, k):
            return first_tile_fills + (tile - 1) * FILLS + k

        def copies(i, engine):
            return sum(p[3] == engine for p in plan[:i])

        def wait_copied(engine, i):
            for name, copied_by in copied.items():
                if copies(i, name):
                    engine.wait_ge(copied_by, copies(i, name))

        def wait_filled(engine, i):
            kind, u, _, _ = plan[i]
            if kind == "lookup":
                engine.wait_ge(chunk_used, CHUNK_BASE[u + 1])
            else:
                engine.wait_ge(turned, sum(p[0] == "turn" for p in plan[:i + 1]))

        block = ctx.enter_context(nc.Block())

        @block.sync
        def _(sp):
            def load_lookup(u):
                at, table, full = u % TABLE_BUFS, tables[LOOKED_UP[u]], CHUNKS[u] - 1
                if u >= TABLE_BUFS:
                    sp.wait_ge(onehot_act, ACT_CHUNKS * (u - TABLE_BUFS + 1))
                    sp.wait_ge(low_split, u - TABLE_BUFS + 1)
                sp.dma_start(lookup_ids_sb[:, at, :], lookup_ids[u:u + 1, :].to_broadcast([P, B])).then_inc(
                    lookup_ids_loaded[u], 16)
                sp.dma_start(table_sb[:, at, 0:full, :], table[0:full * P, :].rearrange(
                    "(p c) d -> p c d", c=full)).then_inc(table_loaded[u], 16)
                sp.dma_start(table_sb[0:chunk_rows(u, full), at, full, :],
                             table[full * P:, :]).then_inc(table_loaded[u], 16)

            sp.dma_start(ids_sb[:, :, :], ids).then_inc(ids_loaded, 16)
            sp.dma_start(row_ids_sb[:, :], row_ids).then_inc(row_ids_loaded, 16)
            load_lookup(0)
            sp.dma_start(ident_sb[:, :], ident).then_inc(ident_loaded, 16)
            sp.dma_start(dense_sb[:, :, :], dense).then_inc(dense_loaded, 16)
            for u in range(1, TABLE_BUFS):
                load_lookup(u)
            sp.dma_start(mask_sb[:, :], low_mask).then_inc(mask_loaded, 16)
            sp.dma_start(w1d_sb[:, :, :], w1_dense).then_inc(w1d_loaded, 16)
            sp.dma_start(b1_sb[:, :], b1).then_inc(small_loaded, 16)
            sp.dma_start(b2_sb[:, :], b2).then_inc(small_loaded, 16)
            sp.dma_start(w3_sb[:, :], w3).then_inc(small_loaded, 16)
            for u in range(TABLE_BUFS, LOOKUPS):
                load_lookup(u)
            sp.dma_start(w1p_sb[:, :, :], w1_pairs).then_inc(w1p_loaded, 16)
            sp.dma_start(w2_sb[:, :, :], w2).then_inc(w2_loaded, 16)
            sp.wait_ge(y_copied, TILES)
            sp.dma_start(out, y_sb[:, :]).then_inc(y_stored, 16)
            sp.wait_ge(y_stored, 16)

        @block.gpsimd
        def _(pool):
            pool.wait_ge(ids_loaded, 16)
            for tile in range(TILES):
                for k in range(FILLS):
                    for slot in FILL_SLOTS[k]:
                        if slot != DENSE_SLOT:
                            f = SLOT_FEATURES[slot] - 1
                            pool.indirect_dma_start(
                                out=rows_sb[:, tile, GATHERED.index(f), :], out_offset=None, in_=tables[f],
                                in_offset=bass.IndirectOffsetOnAxis(
                                    ids_sb[:, tile, f:f + 1].bitcast(UINT32), 0),
                            ).then_inc(rows_gathered[tile][k], 16)

        @block.tensor
        def _(pe):
            def fill(i):
                kind, tile, k, _ = plan[i]
                if i >= 2:
                    engine = plan[i - 2][3]
                    pe.wait_ge(copied[engine], copies(i - 1, engine))
                if kind == "lookup":
                    lookup(tile, turn_ps[i % 2][:, :, :].rearrange("p n b -> p (n b)"))
                else:
                    transposes(tile, k, turn_ps[i % 2])

            def transposes(tile, k, bank):
                if tile == 0 and k == 0:
                    pe.wait_ge(ident_loaded, 16)
                    pe.wait_ge(dense_loaded, 16)
                if gathers := sum(slot != DENSE_SLOT for slot in FILL_SLOTS[k]):
                    pe.wait_ge(rows_gathered[tile][k], 16 * gathers)
                for n, slot in enumerate(FILL_SLOTS[k]):
                    rows = dense_sb[:, tile, :] if slot == DENSE_SLOT else \
                        rows_sb[:, tile, slot - DENSE_SLOT - 1, :]
                    last = nc.tensor.transpose(bank[:, n, :], rows, ident_sb[:, :])
                last.then_inc(turned, 1)

            def lookup(u, bank):
                pe.wait_ge(high_split, u + 1)
                pe.wait_ge(low_split, u + 1)
                for c in range(CHUNKS[u]):
                    for part, chunks in enumerate(dve_chunks(u)):
                        if c == chunks[0]:
                            pe.wait_ge(onehot_dve, 2 * u + part + 1)
                    if c >= CHUNKS[u] - ACT_CHUNKS:
                        pe.wait_ge(onehot_act, ACT_CHUNKS * (u + 1) - (CHUNKS[u] - 1 - c))
                    rows = chunk_rows(u, c)
                    picked = onehot_sb[0:rows, (CHUNK_BASE[u] + c) % ONEHOTS, :]
                    nc.tensor.matmul(bank, high_sb[0:rows, u % 2, c, :], picked, start=c == 0, stop=False)
                    nc.tensor.matmul(bank, low_sb[0:rows, u % 2, c, :], picked,
                                     start=False, stop=c == CHUNKS[u] - 1).then_inc(chunk_used, 1)

            def gram_round(tile, r):
                i = tile * ROUNDS + r
                if i >= 2:
                    pe.wait_ge(low_taken, i - 1)
                for g in range(ROUND):
                    b = tile * P + (r * ROUND + g) * GROUP
                    c = g % GROUPS_PER_BANK * GROUP * N
                    last = nc.tensor.matmul(
                        gram_ps[i % 2][:, g // GROUPS_PER_BANK, c:c + GROUP * N],
                        feats[:, b:b + GROUP, :], feats[:, b:b + GROUP, 0:N], start=True, stop=True)
                last.then_inc(gram_done, 1)

            def layer1(tile):
                cols = slice(tile * P, (tile + 1) * P)
                if tile == 0:
                    pe.wait_ge(w1p_loaded, 16)
                    pe.wait_ge(w1d_summed, 1)
                else:
                    pe.wait_ge(h1_relu, F1 * tile)
                pe.wait_ge(placed_dve, (tile + 1) * ROUNDS)
                pe.wait_ge(placed_act, (tile + 1) * ROUNDS)
                for f in range(F1):
                    fs = slice(f * P, (f + 1) * P)
                    nc.tensor.matmul(h1_ps[:, f, :], w1d_sb[:, 0, fs], feats[:, cols, DENSE_SLOT],
                                     start=True, stop=False)
                    for s in range(VEC_SLOTS):
                        k = min(QUADS, VECS - s * QUADS) * NPAD
                        last = nc.tensor.matmul(h1_ps[:, f, :], w1p_sb[0:k, s, fs], pairs[0:k, s, cols],
                                                start=False, stop=s == VEC_SLOTS - 1)
                last.then_inc(h1_done, 1)

            def layer2(tile):
                if tile == 0:
                    pe.wait_ge(w2_loaded, 16)
                else:
                    pe.wait_ge(h2_relu, tile)
                    pe.wait_ge(y_copied, tile)
                for c in range(F2):
                    for f in range(F1):
                        if c == 0:
                            pe.wait_ge(h1_relu, F1 * tile + f + 1)
                        last = nc.tensor.matmul(h2_ps[:, c, :], w2_sb[:, f, c * P:(c + 1) * P], h1_sb[:, f, :],
                                                start=f == 0, stop=f == F1 - 1)
                last.then_inc(h2_done, 1)

            def layer3(tile):
                pe.wait_ge(h2_relu, tile + 1)
                if tile == 0:
                    pe.wait_ge(small_loaded, 48)
                for c in range(F2):
                    last = nc.tensor.matmul(y_ps, w3_sb[:, c:c + 1], h2_sb[:, c, :],
                                            start=c == 0, stop=c == F2 - 1)
                last.then_inc(y_done, 1)

            for i in range(first_tile_fills):
                fill(i)
            pe.wait_ge(slots_zeroed, 1)
            mlp = [layer1, layer2, layer3]
            for tile in range(TILES):
                wait_copied(pe, plan_index(tile + 1, 0))
                for r in range(max(ROUNDS, FILLS)):
                    if r < ROUNDS:
                        gram_round(tile, r)
                    if tile > 0 and r < len(mlp):
                        mlp[r](tile - 1)
                    if tile + 1 < TILES and r < FILLS:
                        fill(plan_index(tile + 1, r))
            for layer in mlp:
                layer(TILES - 1)

        def copy_fill(copy, i):
            kind, tile, k, _ = plan[i]
            if kind == "lookup":
                return copy(feats[:, :, tile], turn_ps[i % 2][:, :, :].rearrange("p n b -> p (n b)"))
            slots = FILL_SLOTS[k]
            return copy(feats[:, tile * P:(tile + 1) * P, slots.start:slots.stop].rearrange("p b n -> p n b"),
                        turn_ps[i % 2][:, 0:len(slots), :])

        def gram_columns(i, quad, first, count):
            at = gram_ps[i % 2][quad * NPAD:(quad + 1) * NPAD, :, 0:GROUPS_PER_BANK * GROUP * N]
            at = at.rearrange("p k (g c) -> p k g c", c=GROUP * N)
            return at[:, :, :, quad * N + first:quad * N + first + count]

        def vec_places(i, quad, last):
            tile, r = divmod(i, ROUNDS)
            at = vecs[quad * NPAD:(quad + 1) * NPAD, tile % 2, 0:last, r * ROUND:(r + 1) * ROUND]
            return at.rearrange("p t (k g) -> p k g t", k=ROUND_BANKS)

        def place(copy, placed, tile, r, quads):
            b = tile * P + r * ROUND * GROUP
            for to in quads:
                slots = len(range(to, VECS, QUADS))
                for q in range(QUADS):
                    last = copy(pairs[to * NPAD:(to + 1) * NPAD, 0:slots, b + q:b + ROUND * GROUP:GROUP],
                                vecs[q * NPAD:(q + 1) * NPAD, tile % 2, to:VECS:QUADS, r * ROUND:(r + 1) * ROUND])
            last.then_inc(placed, 1)

        @block.scalar
        def _(act):
            def fill(i):
                if plan[i][3] == "act":
                    wait_filled(act, i)
                    copy_fill(nc.scalar.copy, i).then_inc(copied_act, 1)

            def prepare(u):
                at, full, rest = u % TABLE_BUFS, CHUNKS[u] - 1, chunk_rows(u, CHUNKS[u] - 1)
                act.wait_ge(lookup_ids_loaded[u], 16)
                if u >= LOOKUP_PS:
                    act.wait_ge(onehot_dve, 2 * (u - LOOKUP_PS + 1))
                nc.scalar.copy(ids_ps[:, u % LOOKUP_PS, :], lookup_ids_sb[:, at, :]).then_inc(ids_in_psum, 1)
                act.wait_ge(table_loaded[u], 32)
                if u >= 2:
                    act.wait_ge(chunk_used, CHUNK_BASE[u - 1])
                nc.scalar.copy(high_sb[:, u % 2, 0:full, :], table_sb[:, at, 0:full, :])
                nc.scalar.copy(high_sb[0:rest, u % 2, full, :], table_sb[0:rest, at, full, :]).then_inc(high_split, 1)
                if u == 0:
                    act.wait_ge(row_ids_loaded, 16)
                for s in range(ACT_CHUNKS):
                    c = CHUNKS[u] - ACT_CHUNKS + s
                    row = CHUNK_BASE[u] + c
                    nc.scalar.activation(distance_sb[:, s, :], lookup_ids_sb[:, at, :], ACT.Abs,
                                         bias=row_ids_sb[:, row:row + 1], scale=-1.0).then_inc(distance_made, 1)
                    act.wait_ge(distance_made, u * ACT_CHUNKS + s + 1)
                    if row >= ONEHOTS:
                        act.wait_ge(chunk_used, row - ONEHOTS + 1)
                    nc.scalar.activation(onehot_sb[:, row % ONEHOTS, :], distance_sb[:, s, :], ACT.Relu,
                                         bias=1.0, scale=-1.0).then_inc(onehot_act, 1)

            def take_high(tile, r):
                i = tile * ROUNDS + r
                act.wait_ge(gram_done, i + 1)
                if r == 0 and tile >= 2:
                    act.wait_ge(placed_dve, (tile - 1) * ROUNDS)
                for q in range(QUADS):
                    last = nc.scalar.copy(vec_places(i, q, VECS), gram_columns(i, q, HALF, VECS))
                last.then_inc(high_taken, 1)

            def place_part(tile, r):
                act.wait_ge(low_taken, tile * ROUNDS + r + 1)
                place(nc.scalar.copy, placed_act, tile, r, range(QUADS - ACT_QUADS, QUADS))

            def copy_y(tile):
                act.wait_ge(y_done, tile + 1)
                nc.scalar.copy(y_sb[:, tile * P:(tile + 1) * P], y_ps).then_inc(y_copied, 1)

            prepare(0)
            prepare(1)
            for i in range(first_tile_fills):
                fill(i)
                if plan[i][0] == "lookup" and plan[i][1] + 2 < LOOKUPS:
                    prepare(plan[i][1] + 2)
            for tile in range(TILES):
                for r in range(max(ROUNDS, FILLS)):
                    if r < ROUNDS:
                        take_high(tile, r)
                    if 0 < r <= ROUNDS:
                        place_part(tile, r - 1)
                    if tile > 0 and r == 2:
                        copy_y(tile - 1)
                    if tile + 1 < TILES and r < FILLS:
                        fill(plan_index(tile + 1, r))
            copy_y(TILES - 1)

        @block.vector
        def _(dve):
            def fill(i):
                if plan[i][3] == "dve":
                    wait_filled(dve, i)
                    copy_fill(nc.vector.tensor_copy, i).then_inc(copied_dve, 1)

            def prepare(u):
                at, full, rest = u % TABLE_BUFS, CHUNKS[u] - 1, chunk_rows(u, CHUNKS[u] - 1)
                dve.wait_ge(ids_in_psum, u + 1)
                for part, chunks in enumerate(dve_chunks(u)):
                    first, end = CHUNK_BASE[u] + chunks[0], CHUNK_BASE[u] + chunks[-1] + 1
                    if end > ONEHOTS:
                        dve.wait_ge(chunk_used, end - ONEHOTS)
                    for a, b in ring_runs(first, end):
                        shape = [P, b - a, B]
                        last = nc.vector.tensor_tensor(
                            onehot_sb[:, a % ONEHOTS:a % ONEHOTS + b - a, :],
                            ids_ps[:, u % LOOKUP_PS, :].unsqueeze(1).to_broadcast(shape),
                            row_ids_sb[:, a:b].unsqueeze(2).to_broadcast(shape), ALU.is_equal)
                    last.then_inc(onehot_dve, 1)
                    if part == 0:
                        dve.wait_ge(high_split, u + 1)
                        nc.vector.tensor_tensor(low_sb[:, u % 2, 0:full, :], table_sb[:, at, 0:full, :],
                                                high_sb[:, u % 2, 0:full, :].bitcast(FP32), ALU.subtract)
                        nc.vector.tensor_tensor(low_sb[0:rest, u % 2, full, :], table_sb[0:rest, at, full, :],
                                                high_sb[0:rest, u % 2, full, :].bitcast(FP32),
                                                ALU.subtract).then_inc(low_split, 1)

            def take_low(tile, r):
                i = tile * ROUNDS + r
                dve.wait_ge(high_taken, i + 1)
                for q in range(QUADS):
                    where = mask_sb[q * NPAD:(q + 1) * NPAD, :].unsqueeze(1).unsqueeze(1)
                    where = where.to_broadcast([NPAD, ROUND_BANKS, GROUPS_PER_BANK, HALF])
                    last = nc.vector.copy_predicated(vec_places(i, q, HALF), where,
                                                     gram_columns(i, q, 0, HALF))
                last.then_inc(low_taken, 1)

            def place_part(tile, r):
                dve.wait_ge(low_taken, tile * ROUNDS + r + 1)
                place(nc.vector.tensor_copy, placed_dve, tile, r, range(QUADS - ACT_QUADS))

            def relu1(tile):
                dve.wait_ge(h1_done, tile + 1)
                if tile == 0:
                    dve.wait_ge(small_loaded, 48)
                else:
                    dve.wait_ge(h2_done, tile)
                for f in range(F1):
                    nc.vector.tensor_scalar(h1_sb[:, f, :], h1_ps[:, f, :], b1_sb[:, f:f + 1], 0.0,
                                            ALU.add, ALU.max).then_inc(h1_relu, 1)

            def relu2(tile):
                dve.wait_ge(h2_done, tile + 1)
                if tile > 0:
                    dve.wait_ge(y_done, tile)
                for c in range(F2):
                    last = nc.vector.tensor_scalar(h2_sb[:, c, :], h2_ps[:, c, :], b2_sb[:, c:c + 1], 0.0,
                                                   ALU.add, ALU.max)
                last.then_inc(h2_relu, 1)

            nc.vector.memset(feats[:, :, N:NPAD], 0.0).then_inc(slots_zeroed, 1)
            dve.wait_ge(row_ids_loaded, 16)
            for u in range(LOOKUPS):
                prepare(u)
            dve.wait_ge(w1d_loaded, 16)
            nc.vector.tensor_tensor(w1d_sb[:, 0, :], w1d_sb[:, 0, :], w1d_sb[:, 1, :], ALU.add).then_inc(w1d_summed, 1)
            dve.wait_ge(mask_loaded, 16)
            for tile in range(TILES):
                for r in range(max(ROUNDS, FILLS)):
                    if r < ROUNDS:
                        take_low(tile, r)
                        place_part(tile, r)
                    if tile > 0 and r == 0:
                        relu1(tile - 1)
                    if tile > 0 and r == 1:
                        relu2(tile - 1)
                    if tile + 1 < TILES and r < FILLS:
                        fill(plan_index(tile + 1, r))
            relu1(TILES - 1)
            relu2(TILES - 1)


def kernel(**inputs):
    import concourse.bacc as bacc
    from concourse.bass_utils import run_bass_kernel_spmd

    host = {name: np.asarray(a) for name, a in inputs.items()}
    w1 = host["W_top1"]
    w1_padded = np.concatenate([w1, np.zeros((1, H1), w1.dtype)])
    m = np.arange(P)[:, None] % NPAD
    t = np.arange(HALF)[None, :]
    split = lambda a, parts: np.ascontiguousarray(a.reshape(parts, P, -1).transpose(1, 0, 2))
    arrays = {
        "dense": split(host["r_dense_features"], TILES),
        "ids": split(host["ids"], TILES),
        "lookup_ids": np.ascontiguousarray(host["ids"][:, LOOKED_UP].T),
        "row_ids": chunk_row_ids(),
        "w1_pairs": w1_padded[interaction_rows()],
        "w1_dense": np.ascontiguousarray(np.stack([w1[:D], w1[D + PAIRS:]], axis=1)),
        "w2": split(host["W_top2"], F1),
        "w3": np.ascontiguousarray(host["W_top3"].reshape(F2, P).T),
        "b1": np.ascontiguousarray(host["b_top1"].reshape(F1, P).T),
        "b2": np.ascontiguousarray(host["b_top2"].reshape(F2, P).T),
        "ident": np.eye(P, dtype=np.float32),
        "low_mask": ((m > t) & (m <= t + HALF)).astype(np.int32),
    }
    for f in range(TABLES):
        arrays[f"tbl_{f}"] = np.ascontiguousarray(host[f"tbl_{f}"])

    nc = bacc.Bacc("TRN2", target_bir_lowering=False, num_devices=1)
    aps = {name: nc.dram_tensor(f"in_{name}", a.shape, mybir.dt.from_np(a.dtype), kind="ExternalInput").ap()
           for name, a in arrays.items()}
    out = nc.dram_tensor("y", (1, B), FP32, kind="ExternalOutput").ap()
    tables = [aps.pop(f"tbl_{f}") for f in range(TABLES)]
    dlrm_tower(nc, tables=tables, out=out, **aps)
    result = run_bass_kernel_spmd(nc, [{f"in_{name}": a for name, a in arrays.items()}], core_ids=[0])
    return result.results[0]["y"].reshape(B, 1)
```

```python
import numpy as np
import concourse.bass as bass
from concourse import mybir
from contextlib import ExitStack

FP32 = mybir.dt.float32
FP32R = mybir.dt.float32r
BF16 = mybir.dt.bfloat16
INT32 = mybir.dt.int32
UINT32 = mybir.dt.uint32
ACT = mybir.ActivationFunctionType
ALU = mybir.AluOpType

P = 128
B = 512
D = 128
TABLE_ROWS = [1000, 12500, 1250, 1000, 12500, 1250, 1000, 125000, 12500, 1250, 1250, 1250, 1250,
              12500, 1250, 1250, 12500, 12500, 1000, 1250, 12500, 1000, 1250, 12500, 1000, 1250]
TABLES = len(TABLE_ROWS)
N = TABLES + 1
NPAD = 32
H1, H2 = 512, 256
F1, F2 = H1 // P, H2 // P
PAIRS = N * (N - 1) // 2
TILES = B // P
QUADS = P // NPAD

LOOKUP_FROM = [0, 0, 0, 0, 0, 0, 1, 1, 2]
LOOKUPS = len(LOOKUP_FROM)
EARLY_LOOKUPS = LOOKUP_FROM.count(0)
BY_SIZE = sorted(range(TABLES), key=lambda f: TABLE_ROWS[f])
LOOKED_UP = BY_SIZE[:LOOKUPS]
GATHERED = sorted(BY_SIZE[LOOKUPS:])
SLOT_FEATURES = [f + 1 for f in LOOKED_UP] + [0] + [f + 1 for f in GATHERED]
DENSE_SLOT = LOOKUPS

FILL = 4
HALF = (N - 1) // 2
VECS = HALF + 1
VEC_SLOTS = -(-VECS // QUADS)


def gathered_slots(tile):
    return range(sum(first <= tile for first in LOOKUP_FROM), N)


def turn_fills(tile):
    slots = gathered_slots(tile)
    n = -(-len(slots) // FILL)
    return [range(max(slots.start, N - FILL * (n - k)), N - FILL * (n - k - 1)) for k in range(n)]


GATHERS = [(tile, slot) for tile in range(TILES) for slot in gathered_slots(tile) if slot != DENSE_SLOT]
GROUPS = P // QUADS
BANK = 512
GRAM_BANKS = 3
TURN_BANKS = 3
ROUND_GROUPS = 16
ROUNDS = GROUPS // ROUND_GROUPS
CHUNKS = [-(-TABLE_ROWS[f] // P) for f in LOOKED_UP]
CHUNKS_MAX = max(CHUNKS)
CHUNK_BASE = [sum(CHUNKS[:u]) for u in range(LOOKUPS + 1)]
TABLE_BUFS = 3
ONEHOT_MAX = max(n * (B - first * P) for n, first in zip(CHUNKS, LOOKUP_FROM))
WARM_UPS = 18
KEEP_WARM = 4
ACT_QUADS = 1
ACT_CHUNKS = 1


def dve_chunks(u):
    n = CHUNKS[u] - ACT_CHUNKS
    return [range(0, n // 2), range(n // 2, n)]


def chunk_rows(u, c):
    full = CHUNKS[u] - 1
    return P if c < full else TABLE_ROWS[LOOKED_UP[u]] - full * P


def chunk_row_ids():
    p = np.arange(P)
    columns = [p * (CHUNKS[u] - 1) + c if c < CHUNKS[u] - 1 else p + P * c
               for u in range(LOOKUPS) for c in range(CHUNKS[u])]
    return np.stack(columns, axis=1).astype(np.float32)


def pair_row(a, b):
    a, b = min(a, b), max(a, b)
    return D + a * N - a * (a + 1) // 2 + (b - a - 1)


def interaction_rows():
    rows = np.full((P, VEC_SLOTS), D + PAIRS + D)
    for t in range(VECS):
        for m in range(N):
            n = t if t < HALF and t < m <= t + HALF else t + HALF
            if m != n and m != t and (t < HALF or m < HALF):
                rows[(t % QUADS) * NPAD + m, t // QUADS] = pair_row(SLOT_FEATURES[n], SLOT_FEATURES[m])
    return rows


def schedule():
    steps = []

    def prepare(u):
        if u < LOOKUPS:
            steps.append(("prepare", u))

    def lookup(u):
        if u < LOOKUPS:
            steps.append(("lookup", u))

    def turns(tile, first, last):
        steps.extend(("turn", tile, k) for k in range(len(turn_fills(tile)))[first:last])

    def warm():
        steps.append(("warm", sum(kind == "gram" for kind, *_ in steps)))

    early = EARLY_LOOKUPS
    prepare(0)
    prepare(1)
    for k in range(max(early, len(turn_fills(0)))):
        if k < early:
            lookup(k)
            if k + 2 < early:
                prepare(k + 2)
        turns(0, k, k + 1)
        if k == early - 2:
            prepare(early)

    warm()
    steps.append(("gram", 0, 0))
    turns(1, 0, 1)
    steps.append(("gram", 0, 1))
    turns(1, 1, 2)
    steps.append(("last_place", 0))
    prepare(early + 1)
    lookup(early)
    turns(1, 2, 4)
    lookup(early + 1)
    turns(1, 4, None)
    prepare(early + 2)

    for tile in range(1, TILES - 1):
        warm()
        steps.append(("gram", tile, 0))
        turns(tile + 1, 0, 1)
        steps += [("layer1", tile - 1), ("relu1", tile - 1)]
        turns(tile + 1, 1, 2)
        steps += [("gram", tile, 1), ("last_place", tile), ("layer2", tile - 1)]
        if tile == 1:
            lookup(early + 2)
        turns(tile + 1, 2, 3)
        steps.append(("relu2", tile - 1))
        if tile == TILES - 2:
            steps += [("layer1", tile), ("relu1", tile)]
        turns(tile + 1, 3, None)
        steps += [("layer3", tile - 1), ("copy_y", tile - 1)]

    tile = TILES - 1
    warm()
    steps += [("gram", tile, 0), ("gram", tile, 1), ("layer2", tile - 1), ("last_place", tile),
              ("relu2", tile - 1), ("layer1", tile), ("relu1", tile), ("layer3", tile - 1), ("copy_y", tile - 1),
              ("layer2", tile), ("relu2", tile), ("layer3", tile), ("copy_y", tile)]
    return steps


def dlrm_tower(nc, dense, ids, lookup_ids, row_ids, tables, w1_pairs, w1_dense, w2, w3, b1, b2,
               ident, low_mask, out):
    ctx = ExitStack()
    with ctx:
        def sb(name, shape, dt=FP32):
            return ctx.enter_context(nc.sbuf_tensor(name, shape, dt))

        def pb(name, shape):
            return ctx.enter_context(nc.psum_tensor(name, shape, FP32))

        def sem(name):
            return ctx.enter_context(nc.semaphore(name))

        ids_sb = sb("ids_sb", [P, TILES, TABLES], INT32)
        dense_sb = sb("dense_sb", [P, TILES, D])
        rows_sb = sb("rows_sb", [P, len(GATHERS), D])
        table_sb = sb("table_sb", [P, TABLE_BUFS, CHUNKS_MAX, D])
        lookup_ids_sb = sb("lookup_ids_sb", [P, TABLE_BUFS, B], INT32)
        high_sb = sb("high_sb", [P, 2, CHUNKS_MAX, D], FP32R)
        low_sb = sb("low_sb", [P, 2, CHUNKS_MAX, D], FP32R)
        row_ids_sb = sb("row_ids_sb", [P, CHUNK_BASE[LOOKUPS]])
        onehot_sb = sb("onehot_sb", [P, 2, ONEHOT_MAX], FP32R)
        zeros_sb = sb("zeros_sb", [P, BANK], BF16)
        ident_sb = sb("ident_sb", [P, P])
        mask_sb = sb("mask_sb", [P, HALF], INT32)
        w1p_sb = sb("w1p_sb", [P, VEC_SLOTS, H1])
        w1d_sb = sb("w1d_sb", [P, 2, H1])
        w2_sb = sb("w2_sb", [P, F1, H2])
        w3_sb = sb("w3_sb", [P, F2])
        b1_sb = sb("b1_sb", [P, F1])
        b2_sb = sb("b2_sb", [P, F2])
        feats = sb("feats", [P, B, NPAD])
        vecs = sb("vecs", [P, 2, VECS, GROUPS])
        pairs = sb("pairs", [P, VEC_SLOTS, 2, P])
        h1_sb = sb("h1_sb", [P, F1, P])
        h2_sb = sb("h2_sb", [P, F2, P])
        y_sb = table_sb[0:1, 0, 0:B // D, :].rearrange("p c d -> p (c d)")

        turn_ps = [pb(f"turn_ps{i}", [P, FILL, P]) for i in range(TURN_BANKS)]
        gram_ps = [pb(f"gram_ps{i}", [P, BANK]) for i in range(GRAM_BANKS)]
        h1_ps = pb("h1_ps", [P, F1, P])
        tail_ps = pb("tail_ps", [P, BANK])
        h2_ps = tail_ps[:, 0:H2].rearrange("p (f b) -> p f b", f=F2)
        y_ps = tail_ps[0:1, H2:H2 + P]

        def h1_bank(tile, f):
            return turn_ps[0][:, 0, :] if (tile, f) == (TILES - 1, F1 - 1) else h1_ps[:, f, :]

        def h2_bank(tile, c):
            return turn_ps[1][:, 0, :] if (tile, c) == (TILES - 1, F2 - 1) else h2_ps[:, c, :]


        ids_loaded = sem("ids_loaded")
        ident_loaded = sem("ident_loaded")
        dense_loaded = sem("dense_loaded")
        mask_loaded = sem("mask_loaded")
        row_ids_loaded = sem("row_ids_loaded")
        lookup_ids_loaded = [sem(f"lookup_ids_loaded{u}") for u in range(LOOKUPS)]
        table_loaded = [[sem(f"table_loaded{u}_{part}") for part in range(2)] for u in range(LOOKUPS)]
        w1p_loaded = sem("w1p_loaded")
        w1d_loaded = sem("w1d_loaded")
        w2_loaded = sem("w2_loaded")
        small_loaded = sem("small_loaded")
        rows_gathered = [[sem(f"rows_gathered{t}_{k}") for k in range(len(turn_fills(t)))]
                         for t in range(TILES)]
        high_split = sem("high_split")
        low_split = sem("low_split")
        distance_made = sem("distance_made")
        onehot_dve = sem("onehot_dve")
        onehot_act = sem("onehot_act")
        chunk_used = sem("chunk_used")
        slots_zeroed = sem("slots_zeroed")
        zeros_made = sem("zeros_made")
        w1d_summed = sem("w1d_summed")
        turned = sem("turned")
        copied_act = sem("copied_act")
        copied_dve = sem("copied_dve")
        gram_done = sem("gram_done")
        high_taken = sem("high_taken")
        low_taken = sem("low_taken")
        placed_act = sem("placed_act")
        placed_dve = sem("placed_dve")
        h1_done = sem("h1_done")
        h1_relu = sem("h1_relu")
        h2_done = sem("h2_done")
        h2_relu = sem("h2_relu")
        y_done = sem("y_done")
        y_copied = sem("y_copied")
        y_stored = sem("y_stored")

        def onehots(u, chunks):
            rows = B - LOOKUP_FROM[u] * P
            at = onehot_sb[:, u % 2, chunks[0] * rows:(chunks[-1] + 1) * rows]
            return at.rearrange("p (c b) -> p c b", b=rows)

        steps = schedule()
        fills = [step for step in steps if step[0] in ("lookup", "turn")]

        def copier(step):
            if step[0] == "lookup" or step[1] == 0:
                return "act"
            return "act" if step[2] % 2 else "dve"

        copied = {"act": copied_act, "dve": copied_dve}

        def copies(i, engine):
            return sum(copier(step) == engine for step in fills[:i])

        def wait_copied(engine, i):
            for name, copied_by in copied.items():
                if copies(i, name):
                    engine.wait_ge(copied_by, copies(i, name))

        def run(own):
            for kind, *args in steps:
                if kind in own:
                    own[kind](*args)

        def wait_filled(engine, i):
            if fills[i][0] == "lookup":
                engine.wait_ge(chunk_used, CHUNK_BASE[fills[i][1] + 1])
            else:
                engine.wait_ge(turned, sum(kind == "turn" for kind, *_ in fills[:i + 1]))

        block = ctx.enter_context(nc.Block())

        @block.sync
        def _(sp):
            def load_lookup(u):
                at, table, full = u % TABLE_BUFS, tables[LOOKED_UP[u]], CHUNKS[u] - 1
                if u >= TABLE_BUFS:
                    sp.wait_ge(onehot_act, ACT_CHUNKS * (u - TABLE_BUFS + 1))
                    sp.wait_ge(onehot_dve, 2 * (u - TABLE_BUFS + 1))
                    sp.wait_ge(low_split, 2 * (u - TABLE_BUFS + 1))
                sp.dma_start(lookup_ids_sb[:, at, :], lookup_ids[u:u + 1, :].to_broadcast([P, B])).then_inc(
                    lookup_ids_loaded[u], 16)
                by_chunk = table[0:full * P, :].rearrange("(p c) d -> p c d", c=full)
                for part, c in enumerate(dve_chunks(u)):
                    sp.dma_start(table_sb[:, at, c.start:c.stop, :],
                                 by_chunk[:, c.start:c.stop, :]).then_inc(table_loaded[u][part], 16)
                sp.dma_start(table_sb[0:chunk_rows(u, full), at, full, :],
                             table[full * P:, :]).then_inc(table_loaded[u][1], 16)

            sp.dma_start(ids_sb[:, :, :], ids).then_inc(ids_loaded, 16)
            sp.dma_start(row_ids_sb[:, :], row_ids).then_inc(row_ids_loaded, 16)
            load_lookup(0)
            sp.dma_start(ident_sb[:, :], ident).then_inc(ident_loaded, 16)
            sp.dma_start(dense_sb[:, :, :], dense).then_inc(dense_loaded, 16)
            for u in range(1, TABLE_BUFS):
                load_lookup(u)
            sp.dma_start(mask_sb[:, :], low_mask).then_inc(mask_loaded, 16)
            sp.dma_start(w1d_sb[:, :, :], w1_dense).then_inc(w1d_loaded, 16)
            sp.dma_start(b1_sb[:, :], b1).then_inc(small_loaded, 16)
            sp.dma_start(b2_sb[:, :], b2).then_inc(small_loaded, 16)
            sp.dma_start(w3_sb[:, :], w3).then_inc(small_loaded, 16)
            for u in range(TABLE_BUFS, LOOKUPS):
                load_lookup(u)
            sp.dma_start(w1p_sb[:, :, :], w1_pairs).then_inc(w1p_loaded, 16)
            sp.dma_start(w2_sb[:, :, :], w2).then_inc(w2_loaded, 16)
            sp.wait_ge(y_copied, TILES)
            sp.dma_start(out, y_sb[:, :]).then_inc(y_stored, 16)
            sp.wait_ge(y_stored, 16)

        @block.gpsimd
        def _(pool):
            pool.wait_ge(ids_loaded, 16)
            for tile in range(TILES):
                for k, slots in enumerate(turn_fills(tile)):
                    for slot in slots:
                        if slot != DENSE_SLOT:
                            f = SLOT_FEATURES[slot] - 1
                            pool.indirect_dma_start(
                                out=rows_sb[:, GATHERS.index((tile, slot)), :], out_offset=None, in_=tables[f],
                                in_offset=bass.IndirectOffsetOnAxis(
                                    ids_sb[:, tile, f:f + 1].bitcast(UINT32), 0),
                            ).then_inc(rows_gathered[tile][k], 16)

        @block.tensor
        def _(pe):
            def next_bank(step):
                i = fills.index(step)
                if i >= TURN_BANKS:
                    engine = copier(fills[i - TURN_BANKS])
                    pe.wait_ge(copied[engine], copies(i - TURN_BANKS + 1, engine))
                return turn_ps[i % TURN_BANKS]

            def turn(tile, k):
                bank, slots = next_bank(("turn", tile, k)), turn_fills(tile)[k]
                if tile == 0 and k == 0:
                    pe.wait_ge(ident_loaded, 16)
                    pe.wait_ge(dense_loaded, 16)
                if gathers := sum(slot != DENSE_SLOT for slot in slots):
                    pe.wait_ge(rows_gathered[tile][k], 16 * gathers)
                for n, slot in enumerate(slots):
                    rows = dense_sb[:, tile, :] if slot == DENSE_SLOT else rows_sb[:, GATHERS.index((tile, slot)), :]
                    last = nc.tensor.transpose(bank[:, n, :], rows, ident_sb[:, :])
                last.then_inc(turned, 1)

            def lookup(u):
                cols = slice(LOOKUP_FROM[u] * P, B)
                bank = next_bank(("lookup", u))[:, :, :].rearrange("p n b -> p (n b)")[:, cols]
                for c in range(CHUNKS[u]):
                    for part, chunks in enumerate(dve_chunks(u)):
                        if c == chunks[0]:
                            pe.wait_ge(high_split, 2 * u + part + 1)
                            pe.wait_ge(low_split, 2 * u + part + 1)
                            pe.wait_ge(onehot_dve, 2 * u + part + 1)
                    if c >= CHUNKS[u] - ACT_CHUNKS:
                        pe.wait_ge(onehot_act, ACT_CHUNKS * (u + 1) - (CHUNKS[u] - 1 - c))
                    rows = chunk_rows(u, c)
                    picked = onehots(u, [c])[0:rows, 0, :]
                    nc.tensor.matmul(bank, high_sb[0:rows, u % 2, c, :], picked, start=c == 0, stop=False)
                    nc.tensor.matmul(bank, low_sb[0:rows, u % 2, c, :], picked,
                                     start=False, stop=c == CHUNKS[u] - 1).then_inc(chunk_used, 1)

            def gram_round(tile, r):
                i = tile * ROUNDS + r
                if i == 0:
                    pe.wait_ge(slots_zeroed, 1)
                if r == 0:
                    needed = [("lookup", u) for u in range(LOOKUPS) if LOOKUP_FROM[u] <= tile]
                    needed += [("turn", tile, k) for k in range(len(turn_fills(tile)))]
                    wait_copied(pe, 1 + max(fills.index(step) for step in needed))
                if i >= GRAM_BANKS:
                    pe.wait_ge(low_taken, i - GRAM_BANKS + 1)
                for n in range(ROUND_GROUPS):
                    for q in range(QUADS):
                        b = tile * P + q * GROUPS + r * ROUND_GROUPS + n
                        last = nc.tensor.matmul(
                            gram_ps[i % GRAM_BANKS][q * NPAD:(q + 1) * NPAD, n * N:(n + 1) * N],
                            feats[:, b, :], feats[:, b, 0:N], start=True, stop=True)
                last.then_inc(gram_done, 1)

            def layer1(tile):
                cols = slice(tile * P, (tile + 1) * P)
                if tile == 0:
                    pe.wait_ge(w1p_loaded, 16)
                    pe.wait_ge(w1d_summed, 1)
                else:
                    pe.wait_ge(h1_relu, F1 * tile)
                pe.wait_ge(placed_dve, (tile + 1) * ROUNDS)
                pe.wait_ge(placed_act, (tile + 1) * ROUNDS)
                for f in range(F1):
                    fs = slice(f * P, (f + 1) * P)
                    nc.tensor.matmul(h1_bank(tile, f), w1d_sb[:, 0, fs], feats[:, cols, DENSE_SLOT],
                                     start=True, stop=False)
                    for s in range(VEC_SLOTS):
                        k = min(QUADS, VECS - s * QUADS) * NPAD
                        last = nc.tensor.matmul(h1_bank(tile, f), w1p_sb[0:k, s, fs], pairs[0:k, s, tile % 2, :],
                                                start=False, stop=s == VEC_SLOTS - 1)
                    if f >= F1 - 2:
                        last.then_inc(h1_done, 1)

            def layer2(tile):
                if tile == 0:
                    pe.wait_ge(w2_loaded, 16)
                else:
                    pe.wait_ge(h2_relu, F2 * tile)
                    pe.wait_ge(y_copied, tile)
                for c in range(F2):
                    for f in range(F1):
                        if c == 0:
                            pe.wait_ge(h1_relu, F1 * tile + f + 1)
                        last = nc.tensor.matmul(h2_bank(tile, c), w2_sb[:, f, c * P:(c + 1) * P], h1_sb[:, f, :],
                                                start=f == 0, stop=f == F1 - 1)
                    last.then_inc(h2_done, 1)

            def layer3(tile):
                if tile == 0:
                    pe.wait_ge(small_loaded, 48)
                for c in range(F2):
                    pe.wait_ge(h2_relu, F2 * tile + (c + 1 if tile == TILES - 1 else F2))
                    last = nc.tensor.matmul(y_ps, w3_sb[:, c:c + 1], h2_sb[:, c, :],
                                            start=c == 0, stop=c == F2 - 1)
                last.then_inc(y_done, 1)


            def warm(rounds):
                if rounds >= GRAM_BANKS:
                    pe.wait_ge(low_taken, rounds - GRAM_BANKS + 1)
                for _ in range(KEEP_WARM):
                    nc.tensor.matmul(gram_ps[rounds % GRAM_BANKS][:, :], zeros_sb[:, 0:P], zeros_sb[:, :],
                                     start=True, stop=True)

            pe.wait_ge(zeros_made, 1)
            for _ in range(WARM_UPS):
                nc.tensor.matmul(gram_ps[0][:, :], zeros_sb[:, 0:P], zeros_sb[:, :], start=True, stop=True)
            run({"lookup": lookup, "turn": turn, "gram": gram_round, "warm": warm,
                 "layer1": layer1, "layer2": layer2, "layer3": layer3})

        def copy_fill(copy, i):
            kind, which, *k = fills[i]
            if kind == "lookup":
                cols = slice(LOOKUP_FROM[which] * P, B)
                return copy(feats[:, cols, which], turn_ps[i % TURN_BANKS][:, :, :].rearrange("p n b -> p (n b)")[:, cols])
            slots = turn_fills(which)[k[0]]
            return copy(feats[:, which * P:(which + 1) * P, slots.start:slots.stop].rearrange("p b n -> p n b"),
                        turn_ps[i % TURN_BANKS][:, 0:len(slots), :])

        def gram_columns(tile, r, first, count):
            at = gram_ps[(tile * ROUNDS + r) % GRAM_BANKS][:, 0:ROUND_GROUPS * N].rearrange("p (g c) -> p g c", c=N)
            return at[:, :, first:first + count]

        def vec_places(tile, r, last):
            return vecs[:, tile % 2, 0:last, r * ROUND_GROUPS:(r + 1) * ROUND_GROUPS].rearrange("p t g -> p g t")

        def place(engine, copy, placed, tile, r, quads):
            engine.wait_ge(low_taken, tile * ROUNDS + r + 1)
            if r == 0 and tile >= 2:
                engine.wait_ge(h1_done, 2 * (tile - 1))
            first, end = r * ROUND_GROUPS, (r + 1) * ROUND_GROUPS
            for to in quads:
                slots = len(range(to, VECS, QUADS))
                for q in range(QUADS):
                    b = q * GROUPS
                    last = copy(pairs[to * NPAD:(to + 1) * NPAD, 0:slots, tile % 2, b + first:b + end],
                                vecs[q * NPAD:(q + 1) * NPAD, tile % 2, to:VECS:QUADS, first:end])
            last.then_inc(placed, 1)

        @block.scalar
        def _(act):
            def copy_out(*step):
                if copier(step) == "act":
                    i = fills.index(step)
                    wait_filled(act, i)
                    copy_fill(nc.scalar.copy, i).then_inc(copied_act, 1)

            def prepare(u):
                at, full, rest = u % TABLE_BUFS, CHUNKS[u] - 1, chunk_rows(u, CHUNKS[u] - 1)
                cols = slice(LOOKUP_FROM[u] * P, B)
                if u >= 2:
                    act.wait_ge(chunk_used, CHUNK_BASE[u - 1])
                for part, c in enumerate(dve_chunks(u)):
                    act.wait_ge(table_loaded[u][part], 16 * (part + 1))
                    last = nc.scalar.copy(high_sb[:, u % 2, c.start:c.stop, :], table_sb[:, at, c.start:c.stop, :])
                    if part == 1:
                        last = nc.scalar.copy(high_sb[0:rest, u % 2, full, :], table_sb[0:rest, at, full, :])
                    last.then_inc(high_split, 1)
                if u == 0:
                    act.wait_ge(row_ids_loaded, 16)
                act.wait_ge(lookup_ids_loaded[u], 16)
                chunks = range(CHUNKS[u] - ACT_CHUNKS, CHUNKS[u])
                for c in chunks:
                    row = CHUNK_BASE[u] + c
                    nc.scalar.activation(onehots(u, [c])[:, 0, :], lookup_ids_sb[:, at, cols], ACT.Abs,
                                         bias=row_ids_sb[:, row:row + 1], scale=-1.0).then_inc(distance_made, 1)
                for s, c in enumerate(chunks):
                    act.wait_ge(distance_made, u * ACT_CHUNKS + s + 1)
                    picked = onehots(u, [c])[:, 0, :]
                    nc.scalar.activation(picked, picked.bitcast(FP32), ACT.Relu,
                                         bias=1.0, scale=-1.0).then_inc(onehot_act, 1)

            def take_high(tile, r):
                i = tile * ROUNDS + r
                act.wait_ge(gram_done, i + 1)
                if r == 0 and tile >= 2:
                    act.wait_ge(placed_dve, (tile - 1) * ROUNDS)
                nc.scalar.copy(vec_places(tile, r, VECS), gram_columns(tile, r, HALF, VECS)).then_inc(high_taken, 1)
                if r > 0:
                    place_part(tile, r - 1)

            def place_part(tile, r):
                place(act, nc.scalar.copy, placed_act, tile, r, range(QUADS - ACT_QUADS, QUADS))

            def copy_y(tile):
                act.wait_ge(y_done, tile + 1)
                if tile == 0:
                    act.wait_ge(low_split, 2 * LOOKUPS)
                nc.scalar.copy(y_sb[:, tile * P:(tile + 1) * P], y_ps).then_inc(y_copied, 1)

            run({"prepare": prepare, "lookup": lambda u: copy_out("lookup", u),
                 "turn": lambda tile, k: copy_out("turn", tile, k), "gram": take_high,
                 "last_place": lambda tile: place_part(tile, ROUNDS - 1), "copy_y": copy_y})

        @block.vector
        def _(dve):
            def copy_out(*step):
                if copier(step) == "dve":
                    i = fills.index(step)
                    wait_filled(dve, i)
                    copy_fill(nc.vector.tensor_copy, i).then_inc(copied_dve, 1)

            def prepare(u):
                at, full, rest = u % TABLE_BUFS, CHUNKS[u] - 1, chunk_rows(u, CHUNKS[u] - 1)
                cols = slice(LOOKUP_FROM[u] * P, B)
                if u >= 2:
                    dve.wait_ge(chunk_used, CHUNK_BASE[u - 1])
                dve.wait_ge(lookup_ids_loaded[u], 16)
                for part, chunks in enumerate(dve_chunks(u)):
                    for c in chunks:
                        row = CHUNK_BASE[u] + c
                        last = nc.vector.tensor_scalar(onehots(u, [c])[:, 0, :], lookup_ids_sb[:, at, cols],
                                                       row_ids_sb[:, row:row + 1], None, ALU.is_equal)
                    last.then_inc(onehot_dve, 1)
                    dve.wait_ge(high_split, 2 * u + part + 1)
                    first, end = chunks.start, chunks.stop
                    last = nc.vector.tensor_tensor(low_sb[:, u % 2, first:end, :], table_sb[:, at, first:end, :],
                                                   high_sb[:, u % 2, first:end, :].bitcast(FP32), ALU.subtract)
                    if part == 1:
                        last = nc.vector.tensor_tensor(low_sb[0:rest, u % 2, full, :], table_sb[0:rest, at, full, :],
                                                       high_sb[0:rest, u % 2, full, :].bitcast(FP32), ALU.subtract)
                    last.then_inc(low_split, 1)

            def take_low(tile, r):
                i = tile * ROUNDS + r
                if i == 0:
                    dve.wait_ge(w1d_loaded, 16)
                    nc.vector.tensor_tensor(w1d_sb[:, 0, :], w1d_sb[:, 0, :], w1d_sb[:, 1, :],
                                            ALU.add).then_inc(w1d_summed, 1)
                    dve.wait_ge(mask_loaded, 16)
                dve.wait_ge(high_taken, i + 1)
                where = mask_sb[:, :].unsqueeze(1).to_broadcast([P, ROUND_GROUPS, HALF])
                nc.vector.copy_predicated(vec_places(tile, r, HALF), where,
                                          gram_columns(tile, r, 0, HALF)).then_inc(low_taken, 1)
                place(dve, nc.vector.tensor_copy, placed_dve, tile, r, range(QUADS - ACT_QUADS))

            def relu1(tile):
                if tile == 0:
                    dve.wait_ge(small_loaded, 48)
                else:
                    dve.wait_ge(h2_done, F2 * tile)
                for f in range(F1):
                    if f == 0:
                        dve.wait_ge(h1_done, 2 * tile + (1 if tile == TILES - 1 else 2))
                    elif f == F1 - 1:
                        dve.wait_ge(h1_done, 2 * tile + 2)
                    nc.vector.tensor_scalar(h1_sb[:, f, :], h1_bank(tile, f), b1_sb[:, f:f + 1], 0.0,
                                            ALU.add, ALU.max).then_inc(h1_relu, 1)

            def relu2(tile):
                if tile > 0:
                    dve.wait_ge(y_done, tile)
                for c in range(F2):
                    dve.wait_ge(h2_done, F2 * tile + (c + 1 if tile == TILES - 1 else F2))
                    nc.vector.tensor_scalar(h2_sb[:, c, :], h2_bank(tile, c), b2_sb[:, c:c + 1], 0.0,
                                            ALU.add, ALU.max).then_inc(h2_relu, 1)

            nc.vector.memset(zeros_sb[:, :], 0.0).then_inc(zeros_made, 1)
            nc.vector.memset(feats[:, :, N:NPAD], 0.0).then_inc(slots_zeroed, 1)
            dve.wait_ge(row_ids_loaded, 16)
            run({"prepare": prepare, "lookup": lambda u: copy_out("lookup", u),
                 "turn": lambda tile, k: copy_out("turn", tile, k), "gram": take_low,
                 "relu1": relu1, "relu2": relu2})


def kernel(**inputs):
    import concourse.bacc as bacc
    from concourse.bass_utils import run_bass_kernel_spmd

    host = {name: np.asarray(a) for name, a in inputs.items()}
    w1 = host["W_top1"]
    w1_padded = np.concatenate([w1, np.zeros((1, H1), w1.dtype)])
    m = np.arange(P)[:, None] % NPAD
    t = np.arange(HALF)[None, :]
    split = lambda a, parts: np.ascontiguousarray(a.reshape(parts, P, -1).transpose(1, 0, 2))
    arrays = {
        "dense": split(host["r_dense_features"], TILES),
        "ids": split(host["ids"], TILES),
        "lookup_ids": np.ascontiguousarray(host["ids"][:, LOOKED_UP].T),
        "row_ids": chunk_row_ids(),
        "w1_pairs": w1_padded[interaction_rows()],
        "w1_dense": np.ascontiguousarray(np.stack([w1[:D], w1[D + PAIRS:]], axis=1)),
        "w2": split(host["W_top2"], F1),
        "w3": np.ascontiguousarray(host["W_top3"].reshape(F2, P).T),
        "b1": np.ascontiguousarray(host["b_top1"].reshape(F1, P).T),
        "b2": np.ascontiguousarray(host["b_top2"].reshape(F2, P).T),
        "ident": np.eye(P, dtype=np.float32),
        "low_mask": ((m > t) & (m <= t + HALF)).astype(np.int32),
    }
    for f in range(TABLES):
        arrays[f"tbl_{f}"] = np.ascontiguousarray(host[f"tbl_{f}"])

    nc = bacc.Bacc("TRN2", target_bir_lowering=False, num_devices=1)
    aps = {name: nc.dram_tensor(f"in_{name}", a.shape, mybir.dt.from_np(a.dtype), kind="ExternalInput").ap()
           for name, a in arrays.items()}
    out = nc.dram_tensor("y", (1, B), FP32, kind="ExternalOutput").ap()
    tables = [aps.pop(f"tbl_{f}") for f in range(TABLES)]
    dlrm_tower(nc, tables=tables, out=out, **aps)
    result = run_bass_kernel_spmd(nc, [{f"in_{name}": a for name, a in arrays.items()}], core_ids=[0])
    return result.results[0]["y"].reshape(B, 1)
```
